# Optimizing a Trainium2 kernel written in Bass

```python
import numpy as np
import jax
import jax.numpy as jnp

def _softmax(x, axis=-1):
    return jax.nn.softmax(x, axis=axis)

def _gelu(x):
    return jax.nn.gelu(x, approximate=True)

def _silu(x):
    return jax.nn.silu(x)

def _sigmoid(x):
    return jax.nn.sigmoid(x)

def _layernorm(x, axis=-1, eps=1e-05):
    m = jnp.mean(x, axis=axis, keepdims=True)
    v = jnp.var(x, axis=axis, keepdims=True)
    return (x - m) / jnp.sqrt(v + eps)

def _scatter_add(tgt, idx, src, axis=0):
    return tgt.at[idx].add(src)

def _segment_sum(src, seg, n):
    return jax.ops.segment_sum(src, seg, n)
kernel_name = 'mk_xattn_ffn_d2_seqx_r4_72b4b3'

def setup_inputs(seed: int=0):
    np.random.seed(seed)
    _w = jnp.asarray

    def _rec_inputs():
        import jax
        import jax.numpy as jnp
        _rk = jax.random.key(seed)
        x = -0.0002928 + 1 * jax.random.normal(jax.random.fold_in(_rk, 1), (8, 256, 256), jnp.float32)
        _lenS = 256 - jax.random.randint(jax.random.fold_in(_rk, 7), (8,), 0, max(1, 256 // 4) + 1, jnp.int32)
        _lenS2 = 256 - jax.random.randint(jax.random.fold_in(_rk, 8), (8,), 0, max(1, 256 // 4) + 1, jnp.int32)
        _ctx_1024P = jax.random.normal(jax.random.fold_in(_rk, 11), (8, 16, 256), jnp.float32)
        _ctx_1024c = jax.random.dirichlet(jax.random.fold_in(_rk, 511), 0.3 * jnp.ones((16,), jnp.float32), (8, 256))
        _ctx_1024t = jnp.einsum('bsk,bkd->bsd', _ctx_1024c, _ctx_1024P)
        _ctx_1024t = _ctx_1024t * jax.lax.rsqrt(jnp.mean(jnp.square(_ctx_1024t)) + 1e-12) * 0.953939
        ctx_1024 = -1.39393e-06 + 0.999914 * (_ctx_1024t + 0.3 * jax.random.normal(jax.random.fold_in(_rk, 611), (8, 256, 256), jnp.float32))
        fside_Bx16xSxS2_0 = -6.00028e-06 + 0.100001 * jax.random.normal(jax.random.fold_in(_rk, 13), (8, 16, 256, 256), jnp.float32)
        _validS = jnp.arange(256)[None, :] < _lenS[:, None]
        _validS2 = jnp.arange(256)[None, :] < _lenS2[:, None]
        _causal = jnp.tril(jnp.ones((256, 256), dtype=bool))
        mask_Bx1xSxS2_ik1 = jnp.where(jnp.broadcast_to(_validS2[:, None, None, :], (8, 1, 256, 256)), 1, 0).astype(jnp.int32)
        return (x, ctx_1024, fside_Bx16xSxS2_0, mask_Bx1xSxS2_ik1)
    x, ctx_1024, fside_Bx16xSxS2_0, mask_Bx1xSxS2_ik1 = _rec_inputs()

    def _L0_xattn_setup():
        import jax, jax.numpy as jnp
        import numpy as np
        import math
        BS, SEQ, EMBED, HEADS = (2, 512, 256, 16)
        HEAD_DIM = EMBED // HEADS
        key = jax.random.key(seed)
        kq, kk, kv, km, kw, kb = jax.random.split(key, 6)
        q = jax.random.normal(kq, (BS, SEQ, EMBED), dtype=jnp.float32)
        k = jax.random.normal(kk, (BS, SEQ, EMBED), dtype=jnp.float32)
        v = jax.random.normal(kv, (BS, SEQ, EMBED), dtype=jnp.float32)
        padding_mask = jax.random.randint(km, (BS, 1, SEQ, SEQ), 0, 2, dtype=jnp.int32)
        bound = 1.0 / math.sqrt(EMBED)
        W = jax.random.uniform(kw, (EMBED, EMBED), minval=-bound, maxval=bound, dtype=jnp.float32)
        b = jax.random.uniform(kb, (EMBED,), minval=-bound, maxval=bound, dtype=jnp.float32)
        return {'q': q, 'k': k, 'v': v, 'padding_mask': padding_mask, 'W': W, 'b': b}
    _L0_xattn_all = _L0_xattn_setup()
    _L0_xattn_in = {k: v for k, v in _L0_xattn_all.items() if k in ('W', 'b')}
    del _L0_xattn_all

    def _L0_ffn_setup():
        import jax, jax.numpy as jnp
        import numpy as np
        IN_FEATURES = 256
        ACT_BITS = 4

        def _hadamard(size: int) -> np.ndarray:
            h = np.array([[1.0]], dtype=np.float64)
            while h.shape[0] < size:
                h = np.block([[h, h], [h, -h]])
            return (h / np.sqrt(size)).astype(np.float32)

        def _quantize_activations(x, bits=ACT_BITS):
            pos = 2 ** (bits - 1) - 1
            neg = 2 ** (bits - 1)
            scale = jnp.clip(jnp.max(jnp.abs(jax.lax.stop_gradient(x)), axis=-1, keepdims=True), 1e-05) / pos
            q = jnp.clip(jnp.round(x / scale), -neg, pos) * scale
            return x + jax.lax.stop_gradient(q - x)

        def _ternary_quantize_ste(w):
            scale = jnp.clip(jnp.mean(jnp.abs(jax.lax.stop_gradient(w)), axis=1, keepdims=True), 1e-05)
            n = w / scale
            tern = jnp.where(n > 0.5, 1.0, jnp.where(n < -0.5, -1.0, 0.0))
            q = tern * scale
            return w + jax.lax.stop_gradient(q - w)
        key = jax.random.key(seed)
        k1, k2 = jax.random.split(key)
        x = jax.random.normal(k1, (8, 2048, IN_FEATURES), dtype=jnp.float32)
        bound = 1.0 / np.sqrt(IN_FEATURES)
        weight = jax.random.uniform(k2, (256, IN_FEATURES), dtype=jnp.float32, minval=-bound, maxval=bound)
        return {'x': x, 'weight': weight}
    _L0_ffn_all = _L0_ffn_setup()
    _L0_ffn_in = {k: v for k, v in _L0_ffn_all.items() if k in ('weight',)}
    del _L0_ffn_all

    def _L1_xattn_setup():
        import jax, jax.numpy as jnp
        import numpy as np
        import math
        H = 16
        D = 256
        FF = 1024
        DK = D // H
        EPS = 1e-05

        def layer_norm(x, g, b):
            mu = jnp.mean(x, axis=-1, keepdims=True)
            var = jnp.var(x, axis=-1, keepdims=True)
            return (x - mu) * jax.lax.rsqrt(var + EPS) * g + b
        key = jax.random.key(seed)
        ks = jax.random.split(key, 16)
        B, S = (2, 512)
        s = 1.0 / math.sqrt(D)
        return {'x_q': jax.random.normal(ks[0], (B, S, D), jnp.float32), 'x_kv': jax.random.normal(ks[1], (B, S, D), jnp.float32), 'bias': jax.random.normal(ks[2], (B, H, S, S), jnp.float32) * 0.1, 'Wq': jax.random.normal(ks[3], (D, D), jnp.float32) * s, 'Wk': jax.random.normal(ks[4], (D, D), jnp.float32) * s, 'Wv': jax.random.normal(ks[5], (D, D), jnp.float32) * s, 'Wo': jax.random.normal(ks[6], (D, D), jnp.float32) * s, 'W1': jax.random.normal(ks[7], (FF, D), jnp.float32) * s, 'b1': jnp.zeros((FF,), jnp.float32), 'W2': jax.random.normal(ks[8], (D, FF), jnp.float32) * (1.0 / math.sqrt(FF)), 'b2': jnp.zeros((D,), jnp.float32), 'g1': jnp.ones((D,), jnp.float32), 'be1': jnp.zeros((D,), jnp.float32), 'g2': jnp.ones((D,), jnp.float32), 'be2': jnp.zeros((D,), jnp.float32)}
    _L1_xattn_all = _L1_xattn_setup()
    _L1_xattn_in = {k: v for k, v in _L1_xattn_all.items() if k in ('Wq', 'Wk', 'Wv', 'Wo', 'W1', 'b1', 'W2', 'b2', 'g1', 'be1', 'g2', 'be2')}
    del _L1_xattn_all

    def _L1_ffn_setup():
        import jax, jax.numpy as jnp
        import numpy as np
        from math import ceil
        CAPACITY_FACTOR = 2.0
        MIN_CAPACITY = 4
        key = jax.random.key(seed)
        ks = jax.random.split(key, 4)
        B, S, D, Di, E = (4, 512, 256, 1024, 8)
        x = jax.random.normal(ks[0], (B, S, D), dtype=jnp.float32)
        Wr = jax.random.normal(ks[1], (D, E), dtype=jnp.float32) * D ** (-0.5)
        W1 = jax.random.normal(ks[2], (E, D, Di), dtype=jnp.float32) * D ** (-0.5)
        b1 = jnp.zeros((E, Di), dtype=jnp.float32)
        W2 = jax.random.normal(ks[3], (E, Di, D), dtype=jnp.float32) * Di ** (-0.5)
        b2 = jnp.zeros((E, D), dtype=jnp.float32)
        return {'x': x, 'Wr': Wr, 'W1': W1, 'b1': b1, 'W2': W2, 'b2': b2}
    _L1_ffn_all = _L1_ffn_setup()
    _L1_ffn_in = {k: v for k, v in _L1_ffn_all.items() if k in ('Wr', 'W1', 'b1', 'W2', 'b2')}
    del _L1_ffn_all
    return {'x': x, 'ctx_1024': ctx_1024, 'fside_Bx16xSxS2_0': fside_Bx16xSxS2_0, 'mask_Bx1xSxS2_ik1': mask_Bx1xSxS2_ik1, 'L0_xattn_W': _L0_xattn_in['W'], 'L0_xattn_b': _L0_xattn_in['b'], 'L0_ffn_weight': _L0_ffn_in['weight'], 'L1_xattn_Wq': _L1_xattn_in['Wq'], 'L1_xattn_Wk': _L1_xattn_in['Wk'], 'L1_xattn_Wv': _L1_xattn_in['Wv'], 'L1_xattn_Wo': _L1_xattn_in['Wo'], 'L1_xattn_W1': _L1_xattn_in['W1'], 'L1_xattn_b1': _L1_xattn_in['b1'], 'L1_xattn_W2': _L1_xattn_in['W2'], 'L1_xattn_b2': _L1_xattn_in['b2'], 'L1_xattn_g1': _L1_xattn_in['g1'], 'L1_xattn_be1': _L1_xattn_in['be1'], 'L1_xattn_g2': _L1_xattn_in['g2'], 'L1_xattn_be2': _L1_xattn_in['be2'], 'L1_ffn_Wr': _L1_ffn_in['Wr'], 'L1_ffn_W1': _L1_ffn_in['W1'], 'L1_ffn_b1': _L1_ffn_in['b1'], 'L1_ffn_W2': _L1_ffn_in['W2'], 'L1_ffn_b2': _L1_ffn_in['b2']}

def reference(x, ctx_1024, fside_Bx16xSxS2_0, mask_Bx1xSxS2_ik1, L0_xattn_W, L0_xattn_b, L0_ffn_weight, L1_xattn_Wq, L1_xattn_Wk, L1_xattn_Wv, L1_xattn_Wo, L1_xattn_W1, L1_xattn_b1, L1_xattn_W2, L1_xattn_b2, L1_xattn_g1, L1_xattn_be1, L1_xattn_g2, L1_xattn_be2, L1_ffn_Wr, L1_ffn_W1, L1_ffn_b1, L1_ffn_W2, L1_ffn_b2):
    import jax
    import jax.numpy as jnp

    def _L0_xattn_ref(q, k, v, padding_mask, W, b):
        import jax, jax.numpy as jnp
        import numpy as np
        import math
        BS, SEQ, EMBED, HEADS = (2, 512, 256, 16)
        HEAD_DIM = EMBED // HEADS
        bs, seq_len, embed_dim = q.shape
        qr = q.reshape(bs, seq_len, HEADS, HEAD_DIM).transpose(0, 2, 1, 3)
        kr = k.reshape(bs, seq_len, HEADS, HEAD_DIM).transpose(0, 2, 1, 3)
        vr = v.reshape(bs, seq_len, HEADS, HEAD_DIM).transpose(0, 2, 1, 3)
        scale = 1.0 / math.sqrt(HEAD_DIM)
        scores = jnp.einsum('bhqd,bhkd->bhqk', qr, kr) * scale
        scores = jnp.where(padding_mask == 0, jnp.float32(-1000000000.0), scores)
        probs = jax.nn.softmax(scores, axis=-1)
        out = jnp.einsum('bhqk,bhkd->bhqd', probs, vr)
        out = out.transpose(0, 2, 1, 3).reshape(bs, seq_len, embed_dim)
        return out @ W.T + b

    def _L0_ffn_ref(x, weight):
        import jax, jax.numpy as jnp
        import numpy as np
        IN_FEATURES = 256
        ACT_BITS = 4

        def _hadamard(size: int) -> np.ndarray:
            h = np.array([[1.0]], dtype=np.float64)
            while h.shape[0] < size:
                h = np.block([[h, h], [h, -h]])
            return (h / np.sqrt(size)).astype(np.float32)

        def _quantize_activations(x, bits=ACT_BITS):
            pos = 2 ** (bits - 1) - 1
            neg = 2 ** (bits - 1)
            scale = jnp.clip(jnp.max(jnp.abs(jax.lax.stop_gradient(x)), axis=-1, keepdims=True), 1e-05) / pos
            q = jnp.clip(jnp.round(x / scale), -neg, pos) * scale
            return x + jax.lax.stop_gradient(q - x)

        def _ternary_quantize_ste(w):
            scale = jnp.clip(jnp.mean(jnp.abs(jax.lax.stop_gradient(w)), axis=1, keepdims=True), 1e-05)
            n = w / scale
            tern = jnp.where(n > 0.5, 1.0, jnp.where(n < -0.5, -1.0, 0.0))
            q = tern * scale
            return w + jax.lax.stop_gradient(q - w)
        H = jnp.asarray(_hadamard(IN_FEATURES))
        xh = x @ H
        xq = _quantize_activations(xh)
        wq = _ternary_quantize_ste(weight)
        return jnp.einsum('bsi,oi->bso', xq, wq)

    def _L1_xattn_ref(x_q, x_kv, bias, Wq, Wk, Wv, Wo, W1, b1, W2, b2, g1, be1, g2, be2):
        import jax, jax.numpy as jnp
        import numpy as np
        import math
        H = 16
        D = 256
        FF = 1024
        DK = D // H
        EPS = 1e-05

        def layer_norm(x, g, b):
            mu = jnp.mean(x, axis=-1, keepdims=True)
            var = jnp.var(x, axis=-1, keepdims=True)
            return (x - mu) * jax.lax.rsqrt(var + EPS) * g + b
        B, S, _ = x_q.shape

        def split(x):
            return x.reshape(B, -1, H, DK).transpose(0, 2, 1, 3)
        q = split(x_q @ Wq.T)
        k = split(x_kv @ Wk.T)
        v = split(x_kv @ Wv.T)
        scores = jnp.einsum('bhqd,bhkd->bhqk', q, k) / math.sqrt(DK) + bias
        p = jax.nn.softmax(scores, axis=-1)
        o = jnp.einsum('bhqk,bhkd->bhqd', p, v)
        o = o.transpose(0, 2, 1, 3).reshape(B, S, D)
        x = x_q + o @ Wo.T
        h = jax.nn.gelu(layer_norm(x, g1, be1) @ W1.T + b1, approximate=False)
        x = x + h @ W2.T + b2
        return layer_norm(x, g2, be2)

    def _L1_ffn_ref(x, Wr, W1, b1, W2, b2):
        import jax, jax.numpy as jnp
        import numpy as np
        from math import ceil
        CAPACITY_FACTOR = 2.0
        MIN_CAPACITY = 4
        B, S, D = x.shape
        E = Wr.shape[1]
        N = B * S
        k = max(MIN_CAPACITY, ceil(N * CAPACITY_FACTOR / E))
        xt = x.reshape(N, D)
        scores = jax.nn.softmax(xt @ Wr, axis=-1)
        G, idx = jax.lax.top_k(scores.T, k)
        X_in = xt[idx]
        h = jax.nn.gelu(jnp.einsum('ekd,edh->ekh', X_in, W1) + b1[:, None, :], approximate=False)
        X_e = jnp.einsum('ekh,ehd->ekd', h, W2) + b2[:, None, :]
        contrib = (G[..., None] * X_e).reshape(E * k, D)
        out = jnp.zeros((N, D), dtype=x.dtype).at[idx.reshape(-1)].add(contrib)
        return out.reshape(B, S, D)
    x = x + _L0_xattn_ref(_layernorm(x, axis=-1), ctx_1024, ctx_1024, mask_Bx1xSxS2_ik1, L0_xattn_W, L0_xattn_b)
    x = x + _L0_ffn_ref(_layernorm(x, axis=-1), L0_ffn_weight)
    x = x + _L1_xattn_ref(_layernorm(x, axis=-1), ctx_1024, fside_Bx16xSxS2_0, L1_xattn_Wq, L1_xattn_Wk, L1_xattn_Wv, L1_xattn_Wo, L1_xattn_W1, L1_xattn_b1, L1_xattn_W2, L1_xattn_b2, L1_xattn_g1, L1_xattn_be1, L1_xattn_g2, L1_xattn_be2)
    x = x + _L1_ffn_ref(_layernorm(x, axis=-1), L1_ffn_Wr, L1_ffn_W1, L1_ffn_b1, L1_ffn_W2, L1_ffn_b2)
    return x

_drawn_inputs = setup_inputs


def setup_inputs(seed=0):
    import zlib

    import numpy as np

    out = dict(_drawn_inputs(seed))
    spreads = {'L1_xattn_b1': (0.0, 0.273),
     'L1_xattn_b2': (0.0, 0.1),
     'L1_xattn_g1': (1.0, 0.2),
     'L1_xattn_be1': (0.0, 0.1),
     'L1_xattn_g2': (1.0, 0.2),
     'L1_xattn_be2': (0.0, 0.1),
     'L1_ffn_b1': (0.0, 0.549),
     'L1_ffn_b2': (0.0, 0.375)}
    factors = {'fside_Bx16xSxS2_0': 8.0}
    for name, (base, spread) in spreads.items():
        noise = np.random.default_rng([zlib.crc32(name.encode()), seed]).standard_normal(out[name].shape)
        drawn = base * np.exp(spread * noise) if base else spread * noise
        out[name] = jnp.asarray(drawn.astype(out[name].dtype))
    for name, factor in factors.items():
        out[name] = (out[name] * factor).astype(out[name].dtype)
    return out
```

```python
from contextlib import ExitStack

import numpy as np

import concourse.bass as bass
from concourse import mybir

ALU = mybir.AluOpType
ACT = mybir.ActivationFunctionType
AX_X = mybir.AxisListType.X
F32 = mybir.dt.float32
BF16 = mybir.dt.bfloat16
FP16 = mybir.dt.float16
I32 = mybir.dt.int32
U32 = mybir.dt.uint32

P = 128
NB, SEQ, D = 8, 256, 256
H, DK = 16, 16
QT = SEQ // P
DC = D // P
FF = 1024
FC = FF // P
NTILE = NB * QT
E = 8
CAP = max(4, -(-NB * SEQ * 2 // E))
ST = CAP // P
PAIRS = H // 2
UNITS = QT * PAIRS
VW = 3 * DK + 1
EPS = 1e-5
MASKED = -1e30
ROUND = 12582912.0
NBITS = 30
A, C = "A", "C"


class Segment:

    def __init__(self, kind, b, base):
        self.kind, self.b, self.base = kind, b, base


def seg_a(b):
    return Segment(A, b, 0 if isinstance(b, int) and b == 0 else b * 32 - 16)


def seg_c(b):
    return Segment(C, b, 240 if isinstance(b, int) and b == NB - 1 else b * 32 + 32)


def wait(eng, sem, value):
    if not (isinstance(value, int) and value <= 0):
        eng.wait_ge(sem, value)


def build(nc, a, out):
    with ExitStack() as ctx:
        def sb(name, shape, dt=F32):
            return ctx.enter_context(nc.sbuf_tensor(name, shape, dt))

        def psum(name, shape=(P, 512), dt=F32):
            return ctx.enter_context(nc.psum_tensor(name, list(shape), dt))

        def sem(name):
            return ctx.enter_context(nc.semaphore(name))

        normed_dram = nc.dram_tensor("normed_dram", [NB * SEQ, D], F32).ap()

        x_all = sb("x_all", [P, NTILE, D])
        bias_t = [sb(f"bias_t{i}", [P, H, SEQ]) for i in range(QT)]
        ctxT = {k: sb(f"ctxT_{k}", [P, DC, SEQ]) for k in (A, C)}
        v_raw = {k: sb(f"v_raw_{k}", [P, QT, D]) for k in (A, C)}
        v_rest = {k: sb(f"v_rest_{k}", [P, QT, D]) for k in (A, C)}
        v_parts = {k: sb(f"v_parts_{k}", [P, QT, H, VW], BF16) for k in (A, C)}
        mask_int = sb("mask_int", [P, QT, SEQ], I32)
        mask_add = sb("mask_add", [P, QT, SEQ])
        q_even = {k: sb(f"q_even_{k}", [P, DC, SEQ]) for k in (A, C)}
        q_odd = {k: sb(f"q_odd_{k}", [P, DC, SEQ]) for k in (A, C)}
        k_c = sb("k_c", [P, DC, SEQ])
        keyT = {A: ctxT[A], C: k_c}
        neg = sb("neg", [P, 4, 2, SEQ])
        neg_max = sb("neg_max", [P, 4, 2])
        probs = sb("probs", [P, 2, 2, SEQ])
        p_hi = sb("p_hi", [P, 2, 512], FP16)
        p_lo = sb("p_lo", [P, 2, 512], FP16)
        o_raw = sb("o_raw", [P, 2, 8, VW])
        o_sum = sb("o_sum", [P, 2, 8, DK])
        o_inv = sb("o_inv", [P, 2, 8, 1])
        attn = {k: sb(f"attn_{k}", [P, QT, D]) for k in (A, C)}
        attnT = sb("attnT", [P, DC, SEQ])
        nrm = {k: sb(f"nrm_{k}", [P, QT, D]) for k in "ABCFGR"}
        nrmT = sb("nrmT", [P, DC, SEQ])
        nrmT_c = sb("nrmT_c", [P, DC, SEQ])
        xq_res = sb("xq_res", [P, QT, D])
        y_attn = sb("y_attn", [P, QT, D])
        y_bias = sb("y_bias", [P, QT, D])
        y_ffn = sb("y_ffn", [P, QT, D])
        hidT = sb("hidT", [P, FC, SEQ])
        q_amax = sb("q_amax", [P, QT])
        q_scale = sb("q_scale", [P, QT])
        q_inv = sb("q_inv", [P, QT])
        q_rnd = sb("q_rnd", [P, QT, D])
        q_cap = sb("q_cap", [P, QT, D])
        q_int = sb("q_int", [P, QT, D], BF16)
        q_intT = sb("q_intT", [P, DC, SEQ], BF16)
        y_quant = sb("y_quant", [P, QT, D])
        logits = sb("logits", [P, NTILE, E])

        w_a = sb("w_a", [P, DC, D])
        had = sb("had", [P, DC, D])
        w_q = sb("w_q", [P, DC, D])
        w_k = sb("w_k", [P, DC, D])
        w_v = sb("w_v", [P, DC, D])
        w_o = sb("w_o", [P, DC, D])
        w_b = sb("w_b", [P, DC, D])
        w_b_abs = sb("w_b_abs", [P, DC])
        w_b_scale = sb("w_b_scale", [P, DC])
        w_b_half = sb("w_b_half", [P, DC, 2])
        w_b_pos = sb("w_b_pos", [P, DC, D])
        w_b_negv = sb("w_b_negv", [P, DC, D])
        w_b_tern = sb("w_b_tern", [P, DC, D])
        w_b_ternT = sb("w_b_ternT", [P, DC, D], BF16)
        w_b_bc = sb("w_b_bc", [P, DC, P])
        w_b_row = sb("w_b_row", [P, D])
        w_1 = sb("w_1", [P, DC, FF])
        w_2 = sb("w_2", [P, FC, D])
        w_r = sb("w_r", [P, DC, E])
        cols = sb("cols", [P, 2 + 2 * DC + FC])
        rows = sb("rows", [P, 4, D])
        ident = sb("ident", [P, P])
        ident_b = sb("ident_b", [P, P], BF16)
        half_neg = sb("half_neg", [P, QT])

        st6 = {k: sb(f"st6_{k}", [P, QT, 6]) for k in "ABCFGR"}
        mv = {k: sb(f"mv_{k}", [P, QT, 2]) for k in "ABCFGR"}
        var_eps = {k: sb(f"var_eps_{k}", [P, QT]) for k in "ABCFGR"}
        rstd = {k: sb(f"rstd_{k}", [P, QT]) for k in "ABCFGR"}

        ps_s = [psum(f"ps_s{i}") for i in range(2)]
        ps_t = [psum(f"ps_t{i}") for i in range(2)]
        ps_o = [psum(f"ps_o{i}") for i in range(2)]
        ps_m = [psum(f"ps_m{i}") for i in range(2)]

        ld = {n: sem(f"ld_{n}") for n in ("x0", "x", "w", "const", "ctxT_A", "ctxT_C", "v_A", "mask",
                                          "bias0", "bias1", "w1e", "w2e", "b2e", "moe_const")}
        scores_ready = sem("scores_ready")
        neg_ready = sem("neg_ready")
        exp_ready = sem("exp_ready")
        pt_ready = sem("pt_ready")
        hi_ready = sem("hi_ready")
        lo_ready = sem("lo_ready")
        pv_done = sem("pv_done")
        o_copied = sem("o_copied")
        o_add1 = sem("o_add1")
        o_add2 = sem("o_add2")
        o_inv_ready = sem("o_inv_ready")
        o_ready = sem("o_ready")
        ln_bn = {k: sem(f"ln_{k}_bn") for k in "ABCFGR"}
        ln_stats = {k: sem(f"ln_{k}_stats") for k in "ABCFGR"}
        ln_eps = {k: sem(f"ln_{k}_eps") for k in "ABCFGR"}
        ln_rstd = {k: sem(f"ln_{k}_rstd") for k in "ABCFGR"}
        ln_done = {k: sem(f"ln_{k}_done") for k in "ABCFGR"}
        sems = {n: sem(n) for n in (
            "x_biased", "qa_T", "qa_ready", "mask_ready", "va_step", "va_ready",
            "oa_T", "oa_T_copied", "wa_out", "x1_ready",
            "hb_T", "hb_T_copied", "had_out", "q_step", "q_int_ready", "q_int_T", "q_int_T_copied",
            "tern_out", "yq_ready", "x2_ready",
            "k_out", "kc_ready", "v_out", "v_copied", "vc_step", "vc_ready",
            "xc_T", "xc_T_copied", "q_out", "qc_ready", "xq_kept",
            "oc_T", "oc_T_copied", "wo_out", "y_ready", "yb_ready",
            "z_T", "z_T_copied", "f1_out", "gelu_done", "f2_out", "yf_ready",
            "aff_step", "x3_ready", "xr_T", "xr_T_copied", "logit_out", "logit_ready",
            "stored_x", "stored_n", "const_done", "wb_step", "wb_T", "wb_copied",
            "q_capped", "rt_step", "rt_exp", "rank_step", "rank_count", "sel_out", "slot_out", "slots_ready",
            "onehot_ready", "comp_out", "comp_copied", "idx_ready", "gate_step", "gate_ready",
            "gathered", "xg_T", "xT_c0", "xT_ready", "w1_out", "w1_used", "act_done", "w2_out", "y_added",
            "y_gated", "scattered", "flag_ready",
        )}

        S = sems

        def wait_apart(eng, *counts):
            counts = [(x, v if isinstance(v, int) else eng.to_reg(v)) for x, v in counts]
            eng.wait_ge(ld["const"], 16 * N_CONST)
            for x, v in counts:
                wait(eng, x, v)

        msk_e, msk_o = cols[:, 0:1], cols[:, 1:2]

        def pe_transposes(bank, src, idn, last_sem):
            for c in range(DC):
                for t in range(QT):
                    ins = nc.tensor.matmul(bank[:, (c * QT + t) * P:(c * QT + t + 1) * P],
                                           src[:, t, c * P:(c + 1) * P], idn[:, :],
                                           start=True, stop=True, is_transpose=True)
            ins.then_inc(last_sem, 1)

        def pe_token_major(bank, actT, weight, last_sem):
            for t in range(QT):
                for c in range(DC):
                    ins = nc.tensor.matmul(bank[:, t * D:(t + 1) * D], actT[:, c, t * P:(t + 1) * P],
                                           weight[:, c, :], start=(c == 0), stop=(c == DC - 1))
            ins.then_inc(last_sem, 1)

        def pe_feature_major(bank, actT, weight, last_sem):
            for o in range(DC):
                for c in range(DC):
                    ins = nc.tensor.matmul(bank[:, o * SEQ:(o + 1) * SEQ], weight[:, c, o * P:(o + 1) * P],
                                           actT[:, c, :], start=(c == 0), stop=(c == DC - 1))
            ins.then_inc(last_sem, 1)

        def pe_scores(pe, seg, u):
            g = seg.base + u
            qt, hp = divmod(u, PAIRS)
            c, j = divmod(hp, 4)
            r = slice(32 * j, 32 * j + 32)
            if u == 0 and seg.kind == A:
                wait(pe, ld["ctxT_A"], seg.b * 16 + 16)
                wait(pe, S["qa_ready"], seg.b + 1)
            if u == 0 and seg.kind == C:
                wait(pe, S["kc_ready"], seg.b + 1)
                wait(pe, S["qc_ready"], seg.b + 1)
            wait(pe, neg_ready, g - 1)
            for i, q in enumerate((q_even[seg.kind], q_odd[seg.kind])):
                ins = nc.tensor.matmul(ps_s[u % 2][:, i * SEQ:(i + 1) * SEQ],
                                       q[r, c, qt * P:(qt + 1) * P], keyT[seg.kind][r, c, :],
                                       start=True, stop=True)
            ins.then_inc(scores_ready, 1)

        def pe_prob_transposes(pe, seg, u):
            g = seg.base + u
            wait(pe, exp_ready, g + 1)
            wait(pe, lo_ready, g - 1)
            for i in range(2):
                for kb in range(QT):
                    ins = nc.tensor.matmul(ps_t[u % 2][:, (i * QT + kb) * P:(i * QT + kb + 1) * P],
                                           probs[:, u % 2, i, kb * P:(kb + 1) * P], ident[:, :],
                                           start=True, stop=True, is_transpose=True)
            ins.then_inc(pt_ready, 1)

        def pe_values(pe, seg, u):
            g = seg.base + u
            hp = u % PAIRS
            half = hp // 4
            wait(pe, hi_ready, g + 1)
            wait(pe, lo_ready, g + 1)
            if u == 0:
                wait(pe, S["va_ready"] if seg.kind == A else S["vc_ready"], seg.b + 1)
            if u % 4 == 0:
                wait(pe, o_copied, half_base(seg) + u // 4 - 1)
            for i in range(2):
                col = ((hp % 4) * 2 + i) * VW
                n = 0
                for kb in range(QT):
                    for part in (p_hi, p_lo):
                        ins = nc.tensor.matmul(ps_o[half][:, col:col + VW],
                                               part[:, u % 2, (i * QT + kb) * P:(i * QT + kb + 1) * P],
                                               v_parts[seg.kind][:, kb, 2 * hp + i, :],
                                               start=(n == 0), stop=(n == 3))
                        n += 1
            ins.then_inc(pv_done, 1)

        def pe_side1(pe, s, b, prepare, finish):
            f = b - 1
            if prepare:
                if s == 0:
                    wait(pe, ld["ctxT_C"], b * 16 + 16)
                    wait(pe, S["logit_ready"], b - 1)
                    wait(pe, S["qa_ready"], b + 2 if not (isinstance(b, int) and b >= NB - 1) else NB)
                    pe_feature_major(ps_m[1], ctxT[C], w_k, S["k_out"])
                    wait(pe, S["yq_ready"], b + 1)
                    pe_token_major(ps_m[0], ctxT[C], w_v, S["v_out"])
                if s == 2:
                    wait(pe, ln_done["C"], b + 1)
                    wait(pe, S["kc_ready"], b + 1)
                    pe_transposes(ps_m[1], nrm["C"], ident, S["xc_T"])
                if s == 3:
                    wait(pe, S["xc_T_copied"], b + 1)
                    pe_feature_major(ps_m[1], nrmT_c, w_q, S["q_out"])
            if finish:
                if s == 3:
                    wait(pe, o_ready, S_half_c(f) + 4)
                    wait(pe, S["v_copied"], b + 1 if prepare else b)
                    wait(pe, S["yf_ready"], f)
                    pe_transposes(ps_m[0], attn[C], ident, S["oc_T"])
                if s == 4:
                    wait(pe, S["oc_T_copied"], f + 1)
                    pe_token_major(ps_m[0], attnT, w_o, S["wo_out"])
                if s == 6:
                    wait(pe, ln_done["F"], f + 1)
                    pe_transposes(ps_m[0], nrm["F"], ident, S["z_T"])
                if s in (7, 9):
                    hc0 = 0 if s == 7 else FC // 2
                    if s == 7:
                        wait(pe, S["z_T_copied"], f + 1)
                        wait(pe, S["qc_ready"], b + 1 if prepare else b)
                        wait(pe, S["logit_ready"], f)
                    else:
                        wait(pe, S["gelu_done"], f * 2 + 1)
                    for hc in range(hc0, hc0 + FC // 2):
                        bank = ps_m[(hc // 2) % 2]
                        for c in range(DC):
                            ins = nc.tensor.matmul(bank[:, (hc % 2) * SEQ:(hc % 2 + 1) * SEQ],
                                                   w_1[:, c, hc * P:(hc + 1) * P], nrmT[:, c, :],
                                                   start=(c == 0), stop=(c == DC - 1))
                    ins.then_inc(S["f1_out"], 1)
                if s == 11:
                    wait(pe, S["gelu_done"], f * 2 + 2)
                    for t in range(QT):
                        for hc in range(FC):
                            ins = nc.tensor.matmul(ps_m[0][:, t * D:(t + 1) * D], hidT[:, hc, t * P:(t + 1) * P],
                                                   w_2[:, hc, :], start=(hc == 0), stop=(hc == FC - 1))
                    ins.then_inc(S["f2_out"], 1)

        def pe_side2(pe, s, b, rest, prepare, router):
            r, p, f = b + 1, b + 2, b - 1
            if router:
                if s == 0:
                    wait(pe, ln_done["R"], f + 1)
                    wait(pe, S["gelu_done"], f * 2 + 2)
                    pe_transposes(ps_m[1], nrm["R"], ident, S["xr_T"])
                if s == 1:
                    wait(pe, S["xr_T_copied"], f + 1)
                    for t in range(QT):
                        for c in range(DC):
                            ins = nc.tensor.matmul(ps_m[1][:, t * E:(t + 1) * E], nrmT_c[:, c, t * P:(t + 1) * P],
                                                   w_r[:, c, :], start=(c == 0), stop=(c == DC - 1))
                    ins.then_inc(S["logit_out"], 1)
            if rest:
                if s == 3:
                    wait(pe, o_ready, S_half_a(r) + 4)
                    wait(pe, S["yf_ready"], f + 1)
                    wait(pe, S["v_copied"], b + 1)
                    wait(pe, S["wb_copied"], 2)
                    pe_transposes(ps_m[0], attn[A], ident, S["oa_T"])
                if s == 4:
                    wait(pe, S["oa_T_copied"], r + 1)
                    pe_token_major(ps_m[0], attnT, w_a, S["wa_out"])
                if s == 6:
                    wait(pe, ln_done["B"], r + 1)
                    pe_transposes(ps_m[0], nrm["B"], ident, S["hb_T"])
                if s == 7:
                    wait(pe, S["hb_T_copied"], r + 1)
                    pe_token_major(ps_m[0], nrmT, had, S["had_out"])
                if s == 10:
                    wait(pe, S["q_int_ready"], r + 1)
                    for c in range(DC):
                        for t in range(QT):
                            ins = nc.tensor.matmul(ps_m0_bf16(c * QT + t), q_int[:, t, c * P:(c + 1) * P],
                                                   ident_b[:, :], start=True, stop=True, is_transpose=True)
                    ins.then_inc(S["q_int_T"], 1)
                if s == 11:
                    wait(pe, S["q_int_T_copied"], r + 1)
                    pe_token_major(ps_m[0], q_intT, w_b_ternT, S["tern_out"])
            if prepare and s == 12:
                wait(pe, ln_done["A"], p + 1)
                wait(pe, S["wb_copied"], 2)
                wait(pe, S["logit_ready"], f + 1)
                if isinstance(b, int) and b < 1:
                    wait(pe, S["qc_ready"], b + 1)
                    wait(pe, S["qa_ready"], p)
                pe_transposes(ps_m[1], nrm["A"], ident, S["qa_T"])

        def ps_m0_bf16(i):
            return ps_m[0][:, 0:256].bitcast(BF16)[:, i * P:(i + 1) * P]

        def ve_ln_stats(ve, k, b, src, ready=None):
            wait_apart(ve, *([ready] if ready else []))
            for t in range(QT):
                ins = nc.vector.bn_stats(st6[k][:, t, :], src(t))
            ins.then_inc(ln_bn[k], 1)
            wait_apart(ve, (ln_bn[k], b + 1))
            for t in range(QT):
                ins = nc.vector.bn_aggr(mv[k][:, t, :], st6[k][:, t, :])
            ins.then_inc(ln_stats[k], 1)

        nrm_used = {"A": S["qa_T"], "B": S["hb_T"], "C": S["xc_T"], "F": S["z_T"], "G": S["x3_ready"],
                    "R": S["xr_T"]}

        def ve_ln_apply(ve, k, b, src):
            wait(ve, ln_rstd[k], b + 1)
            wait(ve, nrm_used[k], b)
            for t in range(QT):
                ins = nc.vector.tensor_scalar(nrm[k][:, t, :], src(t), mv[k][:, t, 0:1], rstd[k][:, t:t + 1],
                                              ALU.subtract, ALU.mult)
            ins.then_inc(ln_done[k], 1)

        def xtile(b):
            return lambda t: x_all[:, 2 * b + t, :]

        def xpair(b):
            return x_all[:, bass.ds(2 * b, 2), :]

        def ve_neg_scores(ve, seg, u):
            g = seg.base + u
            qt, hp = divmod(u, PAIRS)
            ready = []
            if u == 0 and seg.kind == A:
                ready = [(S["mask_ready"], seg.b + 1)]
            if hp == 0 and seg.kind == C:
                ready = [(ld[f"bias{qt}"], seg.b * 16 + 16)]
            wait_apart(ve, (scores_ready, g + 1), (exp_ready, g - 3), *ready)
            for i in range(2):
                add = mask_add[:, qt, :] if seg.kind == A else bias_t[qt][:, 2 * hp + i, :]
                ins = nc.vector.tensor_tensor_reduce(neg[:, u % 4, i, :], ps_s[u % 2][:, i * SEQ:(i + 1) * SEQ], add,
                                                     -1.0, 3.0e38, ALU.add, ALU.min, neg_max[:, u % 4, i:i + 1])
            ins.then_inc(neg_ready, 1)

        def ve_low_part(ve, seg, u):
            g = seg.base + u
            wait(ve, hi_ready, g + 1)
            wait(ve, pv_done, g - 1)
            nc.vector.tensor_tensor(p_lo[:, u % 2, :], ps_t[u % 2][:, :], p_hi[:, u % 2, :],
                                    ALU.subtract).then_inc(lo_ready, 1)

        def ve_side1(ve, s, b, prepare, finish):
            f = b - 1
            if prepare:
                if s == 0:
                    ve_ln_stats(ve, "C", b, xtile(b), (S["x2_ready"], b + 1))
                if s == 1:
                    wait(ve, S["xq_kept"], b)
                    ve_ln_apply(ve, "C", b, xtile(b))
            if finish:
                if s == 4:
                    wait(ve, S["wo_out"], f + 1)
                    wait(ve, S["xq_kept"], f + 1)
                    wait(ve, S["yb_ready"], f)
                    nc.vector.tensor_tensor(y_attn[:, :, :], ps_m[0][:, :].rearrange("p (t d) -> p t d", t=QT),
                                            xq_res[:, :, :], ALU.add).then_inc(S["y_ready"], 1)
                    ve_ln_stats(ve, "F", f, lambda t: y_attn[:, t, :], (S["y_ready"], f + 1))
                if s == 5:
                    ve_ln_apply(ve, "F", f, lambda t: y_attn[:, t, :])
                if s == 12:
                    wait(ve, S["f2_out"], f + 1)
                    wait(ve, S["yb_ready"], f + 1)
                    nc.vector.tensor_tensor(y_ffn[:, :, :], ps_m[0][:, :].rearrange("p (t d) -> p t d", t=QT),
                                            y_bias[:, :, :], ALU.add).then_inc(S["yf_ready"], 1)
                    ve_ln_stats(ve, "G", f, lambda t: y_ffn[:, t, :], (S["yf_ready"], f + 1))
                if s == 13:
                    ve_ln_apply(ve, "G", f, lambda t: y_ffn[:, t, :])
                if s == 14:
                    ve_ln_stats(ve, "R", f, xtile(f), (S["x3_ready"], f + 1))
                if s == 15:
                    wait(ve, S["stored_n"], f * 16)
                    ve_ln_apply(ve, "R", f, xtile(f))

        def ve_side2(ve, s, b, rest, prepare, router):
            r, p, f = b + 1, b + 2, b - 1
            if router and s == 2:
                wait(ve, S["logit_out"], f + 1)
                nc.vector.tensor_copy(logits[:, bass.ds(2 * f, 2), :],
                                      ps_m[1][:, 0:QT * E].rearrange("p (t e) -> p t e", t=QT)
                                      ).then_inc(S["logit_ready"], 1)
            if rest:
                if s == 4:
                    wait(ve, S["wa_out"], r + 1)
                    wait(ve, S["x_biased"], r + 1)
                    nc.vector.tensor_tensor(xpair(r), ps_m[0][:, :].rearrange("p (t d) -> p t d", t=QT),
                                            xpair(r), ALU.add).then_inc(S["x1_ready"], 1)
                    ve_ln_stats(ve, "B", r, xtile(r), (S["x1_ready"], r + 1))
                if s == 5:
                    ve_ln_apply(ve, "B", r, xtile(r))
                if s == 8:
                    wait(ve, S["had_out"], r + 1)
                    step = r * 4
                    nc.vector.tensor_reduce(q_amax[:, :], ps_m[0][:, :].rearrange("p (t d) -> p t d", t=QT), AX_X,
                                            ALU.max, apply_absolute_value=True).then_inc(S["q_step"], 1)
                    wait(ve, S["q_step"], step + 1)
                    nc.vector.tensor_scalar(q_scale[:, :], q_amax[:, :], 1e-5, 1.0 / 7.0,
                                            ALU.max, ALU.mult).then_inc(S["q_step"], 1)
                    wait(ve, S["q_step"], step + 2)
                    nc.vector.reciprocal(q_inv[:, :], q_scale[:, :]).then_inc(S["q_step"], 1)
                    wait(ve, S["q_step"], step + 3)
                    for t in range(QT):
                        ins = nc.vector.tensor_scalar(q_rnd[:, t, :], ps_m[0][:, t * D:(t + 1) * D], q_inv[:, t:t + 1],
                                                      ROUND, ALU.mult, ALU.add)
                    ins.then_inc(S["q_step"], 1)
                if s == 9:
                    wait(ve, S["q_step"], r * 4 + 4)
                    nc.vector.tensor_scalar(q_cap[:, :, :], q_rnd[:, :, :], -ROUND, 7.0,
                                            ALU.add, ALU.min).then_inc(S["q_capped"], 1)
                    wait(ve, S["q_capped"], r + 1)
                    wait(ve, S["q_int_T"], r)
                    nc.vector.tensor_scalar(q_int[:, :, :], q_cap[:, :, :], -8.0, None,
                                            ALU.max).then_inc(S["q_int_ready"], 1)
                if s == 12:
                    wait(ve, S["tern_out"], r + 1)
                    wait(ve, S["x2_ready"], r)
                    for t in range(QT):
                        ins = nc.vector.scalar_tensor_tensor(y_quant[:, t, :], ps_m[0][:, t * D:(t + 1) * D],
                                                             q_scale[:, t:t + 1], w_b_row[:, :], ALU.mult, ALU.mult)
                    ins.then_inc(S["yq_ready"], 1)
            if prepare:
                if s == 9:
                    first = isinstance(p, int) and p == 0
                    ve_ln_stats(ve, "A", p, xtile(p), (ld["x0"], 16) if first else (ld["x"], 16))
                if s == 10:
                    ve_ln_apply(ve, "A", p, xtile(p))

        def ve_o_inverse(ve, half, i):
            wait(ve, o_copied, half + 1)
            nc.vector.reciprocal(o_inv[:, i, :, :], o_raw[:, i, :, 3 * DK:VW]).then_inc(o_inv_ready, 1)

        def ac_exp(ac, seg, u):
            g = seg.base + u
            wait(ac, neg_ready, g + 1)
            wait(ac, pt_ready, g - 1)
            for i in range(2):
                ins = nc.scalar.activation(probs[:, u % 2, i, :], neg[:, u % 4, i, :], ACT.Exp,
                                           bias=neg_max[:, u % 4, i:i + 1], scale=-1.0)
            ins.then_inc(exp_ready, 1)

        def ac_high_part(ac, seg, u):
            g = seg.base + u
            wait(ac, pt_ready, g + 1)
            wait(ac, pv_done, g - 1)
            nc.scalar.activation(p_hi[:, u % 2, :], ps_t[u % 2][:, :], ACT.Copy).then_inc(hi_ready, 1)

        def ac_side1(ac, s, b, prepare, finish):
            f = b - 1
            if prepare:
                if s == 0:
                    wait(ac, S["k_out"], b + 1)
                    nc.scalar.copy(k_c[:, :, :].rearrange("p c q -> p (c q)"), ps_m[1][:, :]).then_inc(S["kc_ready"], 1)
                    wait(ac, S["v_out"], b + 1)
                    wait(ac, S["vc_ready"], b)
                    nc.scalar.copy(v_raw[C][:, :, :].rearrange("p c q -> p (c q)"), ps_m[0][:, :]).then_inc(S["v_copied"], 1)
                if s == 2:
                    wait(ac, S["xc_T"], b + 1)
                    nc.scalar.copy(nrmT_c[:, :, :].rearrange("p c q -> p (c q)"), ps_m[1][:, :]).then_inc(S["xc_T_copied"], 1)
                if s == 3:
                    wait(ac, S["q_out"], b + 1)
                    nc.scalar.activation(q_even[C][:, :, :].rearrange("p c q -> p (c q)"), ps_m[1][:, :], ACT.Copy,
                                         scale=msk_e)
                    nc.scalar.activation(q_odd[C][:, :, :].rearrange("p c q -> p (c q)"), ps_m[1][:, :], ACT.Copy,
                                         scale=msk_o).then_inc(S["qc_ready"], 1)
            if finish:
                if s == 3:
                    wait(ac, S["oc_T"], f + 1)
                    nc.scalar.copy(attnT[:, :, :].rearrange("p c q -> p (c q)"), ps_m[0][:, :]).then_inc(S["oc_T_copied"], 1)
                if s == 6:
                    wait(ac, S["z_T"], f + 1)
                    for c in range(DC):
                        ins = nc.scalar.activation(nrmT[:, c, :], ps_m[0][:, c * SEQ:(c + 1) * SEQ], ACT.Identity,
                                                   bias=cols[:, 2 + DC + c:3 + DC + c], scale=cols[:, 2 + c:3 + c])
                    ins.then_inc(S["z_T_copied"], 1)
                if s in (8, 10):
                    hc0 = 0 if s == 8 else FC // 2
                    wait(ac, S["f1_out"], f * 2 + (1 if s == 8 else 2))
                    for hc in range(hc0, hc0 + FC // 2):
                        ins = nc.scalar.activation(hidT[:, hc, :], ps_m[(hc // 2) % 2][:, (hc % 2) * SEQ:(hc % 2 + 1) * SEQ],
                                                   ACT.Gelu, bias=cols[:, 2 + 2 * DC + hc:3 + 2 * DC + hc])
                    ins.then_inc(S["gelu_done"], 1)

        def ac_side2(ac, s, b, rest, prepare, router):
            r, p, f = b + 1, b + 2, b - 1
            if router and s == 0:
                wait(ac, S["xr_T"], f + 1)
                nc.scalar.copy(nrmT_c[:, :, :].rearrange("p c q -> p (c q)"), ps_m[1][:, :]).then_inc(S["xr_T_copied"], 1)
            if rest:
                if s == 3:
                    wait(ac, S["oa_T"], r + 1)
                    nc.scalar.copy(attnT[:, :, :].rearrange("p c q -> p (c q)"), ps_m[0][:, :]).then_inc(S["oa_T_copied"], 1)
                if s == 6:
                    wait(ac, S["hb_T"], r + 1)
                    nc.scalar.copy(nrmT[:, :, :].rearrange("p c q -> p (c q)"), ps_m[0][:, :]).then_inc(S["hb_T_copied"], 1)
                if s == 10:
                    wait(ac, S["q_int_T"], r + 1)
                    nc.scalar.copy(q_intT[:, :, :].rearrange("p c q -> p (c q)"), ps_m[0][:, 0:256].bitcast(BF16)
                                   ).then_inc(S["q_int_T_copied"], 1)
            if prepare and s == 12:
                wait(ac, S["qa_T"], p + 1)
                nc.scalar.activation(q_even[A][:, :, :].rearrange("p c q -> p (c q)"), ps_m[1][:, :], ACT.Copy, scale=msk_e)
                nc.scalar.activation(q_odd[A][:, :, :].rearrange("p c q -> p (c q)"), ps_m[1][:, :], ACT.Copy,
                                     scale=msk_o).then_inc(S["qa_ready"], 1)

        def ac_o_copy(ac, half, i, units):
            wait(ac, pv_done, units)
            wait(ac, o_ready, half - 1)
            nc.scalar.copy(o_raw[:, i, :, :].rearrange("p h v -> p (h v)"), ps_o[i][:, 0:8 * VW]).then_inc(o_copied, 1)

        def po_rstd(po, k, b):
            wait_apart(po, (ln_stats[k], b + 1))
            nc.gpsimd.tensor_scalar(var_eps[k][:, :], mv[k][:, :, 1], EPS, None, ALU.add).then_inc(ln_eps[k], 1)
            wait(po, ln_eps[k], b + 1)
            nc.gpsimd.tensor_tensor(rstd[k][:, :], var_eps[k][:, :], half_neg[:, :], ALU.pow).then_inc(ln_rstd[k], 1)

        def po_split_values(po, k, b, ready, step_sem, ready_sem):
            raw = v_raw[k][:, :, :].rearrange("p t (h d) -> p t h d", h=H)
            rest = v_rest[k][:, :, :].rearrange("p t (h d) -> p t h d", h=H)
            part = [v_parts[k][:, :, :, n * DK:(n + 1) * DK] for n in range(3)]
            wait_apart(po, *ready)
            for t in range(QT):
                ins = nc.gpsimd.tensor_copy(part[0][:, t], raw[:, t])
            ins.then_inc(step_sem, 1)
            wait(po, step_sem, 4 * b + 1)
            for t in range(QT):
                ins = nc.gpsimd.tensor_tensor(rest[:, t], raw[:, t], part[0][:, t], ALU.subtract)
            ins.then_inc(step_sem, 1)
            wait_apart(po, (step_sem, 4 * b + 2))
            for t in range(QT):
                ins = nc.gpsimd.tensor_copy(part[1][:, t], rest[:, t])
            ins.then_inc(step_sem, 1)
            wait(po, step_sem, 4 * b + 3)
            for t in range(QT):
                ins = nc.gpsimd.tensor_tensor(raw[:, t], rest[:, t], part[1][:, t], ALU.subtract)
            ins.then_inc(step_sem, 1)
            wait_apart(po, (step_sem, 4 * b + 4))
            for t in range(QT):
                ins = nc.gpsimd.tensor_copy(part[2][:, t], raw[:, t])
            ins.then_inc(ready_sem, 1)

        def po_side1(po, s, b, prepare, finish):
            f = b - 1
            if prepare:
                if s == 0:
                    po_rstd(po, "C", b)
                if s == 1:
                    ready = ((S["v_copied"], b + 1), (pv_done, seg_c_units(b - 1)))
                    po_split_values(po, C, b, ready, S["vc_step"], S["vc_ready"])
                if s == 6:
                    wait_apart(po, (ln_done["C"], b + 1), (S["y_ready"], b))
                    nc.gpsimd.tensor_copy(xq_res[:, :, :], nrm["C"][:, :, :]).then_inc(S["xq_kept"], 1)
            if finish:
                if s == 4:
                    po_rstd(po, "F", f)
                if s == 5:
                    wait(po, S["yf_ready"], f)
                    nc.gpsimd.tensor_tensor(y_bias[:, :, :], y_attn[:, :, :], rows[:, 1:2, :].to_broadcast([P, QT, D]),
                                            ALU.add).then_inc(S["yb_ready"], 1)
                if s == 12:
                    po_rstd(po, "G", f)
                if s == 13:
                    wait(po, ln_done["G"], f + 1)
                    nc.gpsimd.tensor_tensor(nrm["G"][:, :, :], nrm["G"][:, :, :], rows[:, 2:3, :].to_broadcast([P, QT, D]),
                                            ALU.mult).then_inc(S["aff_step"], 1)
                    wait(po, S["aff_step"], 2 * f + 1)
                    nc.gpsimd.tensor_tensor(nrm["G"][:, :, :], nrm["G"][:, :, :], rows[:, 3:4, :].to_broadcast([P, QT, D]),
                                            ALU.add).then_inc(S["aff_step"], 1)
                    wait(po, S["aff_step"], 2 * f + 2)
                    nc.gpsimd.tensor_tensor(xpair(f), xpair(f), nrm["G"][:, :, :], ALU.add).then_inc(S["x3_ready"], 1)
                if s == 14:
                    po_rstd(po, "R", f)

        def po_side2(po, s, b, rest, prepare, router):
            r, p = b + 1, b + 2
            if rest:
                if s == 4:
                    po_rstd(po, "B", r)
                if s == 12:
                    wait(po, S["yq_ready"], r + 1)
                    nc.gpsimd.tensor_tensor(xpair(r), xpair(r), y_quant[:, :, :], ALU.add).then_inc(S["x2_ready"], 1)
            if prepare:
                if s == 3:
                    wait_apart(po, (ld["mask"], p * 16 + 16), (neg_ready, seg_a_units(p - 1)))
                    nc.gpsimd.tensor_scalar(mask_add[:, :, :], mask_int[:, :, :], 0, MASKED,
                                            ALU.is_equal, ALU.mult).then_inc(S["mask_ready"], 1)
                    ready = ((ld["v_A"], p * 16 + 16), (pv_done, seg_a_units(p - 1)))
                    po_split_values(po, A, p, ready, S["va_step"], S["va_ready"])
                if s == 9:
                    po_rstd(po, "A", p)
                if s == 10:
                    wait(po, ln_done["A"], p + 1)
                    nc.gpsimd.tensor_tensor(xpair(p), xpair(p), rows[:, 0:1, :].to_broadcast([P, QT, D]),
                                            ALU.add).then_inc(S["x_biased"], 1)

        def po_o_normalise(po, half, kind, b, j):
            qt, i = divmod(j, 2)
            wait(po, o_copied, half + 1)
            nc.gpsimd.tensor_tensor(o_sum[:, i, :, :], o_raw[:, i, :, 0:DK], o_raw[:, i, :, DK:2 * DK],
                                    ALU.add).then_inc(o_add1, 1)
            wait(po, o_add1, half + 1)
            nc.gpsimd.tensor_tensor(o_sum[:, i, :, :], o_sum[:, i, :, :], o_raw[:, i, :, 2 * DK:3 * DK],
                                    ALU.add).then_inc(o_add2, 1)
            wait(po, o_add2, half + 1)
            wait(po, o_inv_ready, half + 1)
            if j == 0:
                wait(po, S["oa_T"] if kind == A else S["oc_T"], b)
            dst = attn[kind][:, qt, i * P:(i + 1) * P].rearrange("p (h d) -> p h d", h=8)
            nc.gpsimd.tensor_tensor(dst, o_sum[:, i, :, :], o_inv[:, i, :, :].to_broadcast([P, 8, DK]),
                                    ALU.mult).then_inc(o_ready, 1)

        def S_half_a(b):
            return b * 8 - 4 if not (isinstance(b, int) and b == 0) else 0

        def S_half_c(b):
            return 60 if isinstance(b, int) and b == NB - 1 else b * 8 + 8

        def seg_a_units(b):
            if isinstance(b, int):
                return 0 if b < 0 else seg_a(b).base + UNITS
            return b * 32

        def seg_c_units(b):
            if isinstance(b, int):
                return 0 if b < 0 else seg_c(b).base + UNITS
            return b * 32 + 48

        def half_base(seg):
            return S_half_a(seg.b) if seg.kind == A else S_half_c(seg.b)

        def halves(s, main, prev):
            if s == 1 and prev is not None:
                return half_base(prev) + 3, prev, 3, prev.base + UNITS
            if main is not None and s in (5, 9, 13):
                j = (s - 5) // 4
                return half_base(main) + j, main, j, main.base + 4 * j + 4
            return None

        def walk(main, prev, ahead, nxt, unit_first, unit_slot, tail, half_work, side):
            for s in range(UNITS):
                if main is not None:
                    if s == 0 and not ahead:
                        unit_first(main)
                    unit_slot(main, s, nxt, prev if s == 0 else None)
                elif s == 0 and prev is not None:
                    tail(prev)
                h = halves(s, main, prev)
                if h is not None:
                    half_work(*h)
                side(s)

        def following(main, s, n, nxt):
            if s + n < UNITS:
                return main, s + n
            return (nxt, s + n - UNITS) if nxt is not None else None

        def pe_seg(pe, main, prev, ahead, nxt, side):
            def first(m):
                pe_scores(pe, m, 0)
                pe_scores(pe, m, 1)

            def slot(m, s, nx, pv):
                nu = following(m, s, 2, nx)
                if nu is not None:
                    pe_scores(pe, *nu)
                pe_prob_transposes(pe, m, s)
                if s > 0:
                    pe_values(pe, m, s - 1)
                elif pv is not None:
                    pe_values(pe, pv, UNITS - 1)

            walk(main, prev, ahead, nxt, first, slot, lambda pv: pe_values(pe, pv, UNITS - 1),
                 lambda *h: None, side)

        def ve_seg(ve, main, prev, ahead, nxt, side):
            def first(m):
                ve_neg_scores(ve, m, 0)
                ve_neg_scores(ve, m, 1)

            def slot(m, s, nx, pv):
                nu = following(m, s, 2, nx)
                if nu is not None:
                    ve_neg_scores(ve, *nu)
                ve_low_part(ve, m, s)

            walk(main, prev, ahead, nxt, first, slot, lambda pv: None,
                 lambda half, seg, j, units: ve_o_inverse(ve, half, j % 2), side)

        def ac_seg(ac, main, prev, ahead, nxt, side):
            def slot(m, s, nx, pv):
                nu = following(m, s, 1, nx)
                if nu is not None:
                    ac_exp(ac, *nu)
                ac_high_part(ac, m, s)

            walk(main, prev, ahead, nxt, lambda m: ac_exp(ac, m, 0), slot, lambda pv: None,
                 lambda half, seg, j, units: ac_o_copy(ac, half, j % 2, units), side)

        def po_seg(po, main, prev, ahead, nxt, side):
            walk(main, prev, ahead, nxt, lambda m: None, lambda *x: None, lambda pv: None,
                 lambda half, seg, j, units: po_o_normalise(po, half, seg.kind, seg.b, j), side)

        def layers(eng, engine_seg, side1, side2):
            def iteration(b, finish=True, last_a=False):
                nxt_a = None if last_a else seg_a(b + 2)
                engine_seg(eng, seg_a(b + 1), seg_c(b - 1) if finish else None, finish, seg_c(b),
                           lambda s: side1(eng, s, b, True, finish))
                engine_seg(eng, seg_c(b), seg_a(b + 1), True, nxt_a,
                           lambda s: side2(eng, s, b, True, not last_a, finish))

            for s in range(UNITS):
                side2(eng, s, -2, False, True, False)
            engine_seg(eng, seg_a(0), None, False, None, lambda s: None)
            engine_seg(eng, None, seg_a(0), False, None, lambda s: side2(eng, s, -1, True, True, False))
            iteration(0, finish=False)
            with eng.Fori(1, NB - 2) as b:
                iteration(b)
            iteration(NB - 2, last_a=True)
            b = NB - 1
            engine_seg(eng, None, seg_c(b - 1), False, None, lambda s: side1(eng, s, b, True, True))
            engine_seg(eng, seg_c(b), None, False, None, lambda s: side2(eng, s, b, False, False, True))
            engine_seg(eng, None, seg_c(b), False, None, lambda s: side1(eng, s, NB, False, True))
            for s in range(UNITS):
                side2(eng, s, NB, False, False, True)

        def ve_start(ve):
            done = [0]

            def step(ins):
                ins.then_inc(S["wb_step"], 1)
                done[0] += 1
                ve.wait_ge(S["wb_step"], done[0])

            ve.wait_ge(ld["w"], 16 * N_WEIGHTS)
            step(nc.vector.tensor_reduce(w_b_abs[:, :], w_b[:, :, :], AX_X, ALU.add, apply_absolute_value=True))
            step(nc.vector.tensor_scalar(w_b_scale[:, :], w_b_abs[:, :], 1.0 / D, 1e-5, ALU.mult, ALU.max))
            step(nc.vector.tensor_scalar(w_b_half[:, :, 0], w_b_scale[:, :], 0.5, None, ALU.mult))
            step(nc.vector.tensor_scalar(w_b_half[:, :, 1], w_b_scale[:, :], -0.5, None, ALU.mult))
            for c in range(DC):
                step(nc.vector.tensor_scalar(w_b_pos[:, c, :], w_b[:, c, :], w_b_half[:, c, 0:1], None, ALU.is_gt))
                step(nc.vector.tensor_scalar(w_b_negv[:, c, :], w_b[:, c, :], w_b_half[:, c, 1:2], None, ALU.is_lt))
            for c in range(DC):
                step(nc.vector.tensor_copy(w_b_bc[:, c, :], w_b_scale[:, c:c + 1].to_broadcast([P, P])))
            step(nc.vector.tensor_copy(ident_b[:, :], ident[:, :]))
            step(nc.vector.tensor_tensor(w_b_tern[:, :, :], w_b_pos[:, :, :], w_b_negv[:, :, :], ALU.subtract))

        N_START = 12

        def pe_start(pe):
            pe.wait_ge(S["wb_step"], N_START)
            pe_transposes(ps_m[0], w_b_tern, ident, S["wb_T"])
            for c in range(DC):
                ins = nc.tensor.matmul(ps_m[1][:, c * P:(c + 1) * P], w_b_bc[:, c, :], ident[:, :],
                                       start=True, stop=True)
            ins.then_inc(S["wb_T"], 1)

        def ac_start(ac):
            ac.wait_ge(S["wb_T"], 2)
            nc.scalar.copy(w_b_ternT[:, :, :].rearrange("p c q -> p (c q)"), ps_m[0][:, :]).then_inc(S["wb_copied"], 1)
            nc.scalar.copy(w_b_row[:, :], ps_m[1][:, 0:D]).then_inc(S["wb_copied"], 1)

        def po_start(po):
            nc.gpsimd.memset(half_neg[:, :], -0.5).then_inc(S["const_done"], 1)
            for k in (A, C):
                for t in range(QT):
                    ins = nc.gpsimd.memset(v_parts[k][:, t, :, 3 * DK:VW], 1.0)
            ins.then_inc(S["const_done"], 1)
            po.wait_ge(S["const_done"], 2)

        ones_b, upper_b = sb("ones_b", [P, P], BF16), sb("upper_b", [P, P], BF16)
        rt_max = sb("rt_max", [P, NTILE, 1])
        rt_shift = sb("rt_shift", [P, NTILE, E])
        rt_exp = sb("rt_exp", [P, NTILE, E])
        rt_sum = sb("rt_sum", [P, NTILE, 1])
        rt_inv = sb("rt_inv", [P, NTILE, 1])
        score = sb("score", [P, NTILE, E])
        score_r1 = sb("score_r1", [P, NTILE, E])
        score_r2 = sb("score_r2", [P, NTILE, E])
        bits = sb("bits", [P, NBITS, E], I32)
        cur = sb("cur", [P, 1, E])
        cand = sb("cand", [P, 1, E])
        kept = sb("kept", [P, 1, E])
        count = sb("count", [P, E])
        flag = sb("flag", [P, NTILE, E], BF16)
        above = sb("above", [P, NTILE, E], BF16)
        equal = sb("equal", [P, NTILE, E], BF16)
        room = sb("room", [P, 1, E])
        early = sb("early", [P, NTILE, E])
        tied = sb("tied", [P, NTILE, E])
        chosen = sb("chosen", [P, NTILE, E], BF16)
        slot_1 = sb("slot_1", [P, NTILE, E])
        slot = sb("slot", [P, NTILE, E])
        info = sb("info", [P, NTILE, E, 5], BF16)
        iota = sb("iota", [P, CAP], FP16)
        moe_f32 = sb("moe_f32", [P, 2 * P + CAP + NTILE + 1])
        onehot = bias_t[0][:, :, :].rearrange("p h k -> p (h k)").bitcast(BF16).rearrange("p (t s) -> p t s", t=NTILE)
        hid_e = bias_t[1][:, :, :].rearrange("p h k -> p (h k)").rearrange("p (h s) -> p h s", h=FC)
        comp = sb("comp", [P, ST, 8])
        idx = [sb(f"idx{i}", [P, ST], U32) for i in range(2)]
        gate1 = sb("gate_part", [P, ST])
        gate = [sb(f"gate{i}", [P, ST]) for i in range(2)]
        xg = w_1[:, 0, :].rearrange("p (s d) -> p s d", s=ST)
        xgT = w_1[:, 1, :].rearrange("p (c s) -> p c s", c=DC)
        w1e = neg[:, :, :, :].rearrange("p (c f) i k -> p c (f i k)", c=DC)
        w2e = hidT
        b1e = sb("b1e", [P, E, FC])
        b2e = x_all[:, 0:E, :]
        y_e = w_2[:, 0:ST, :]
        y_g = w_2[:, ST:2 * ST, :]
        ps_h = [ps_s[0], ps_s[1], ps_t[0]]
        ps_c = ps_t[1]

        def tok(ap):
            return ap[:, :, :].rearrange("p t e -> p (t e)")

        def every_tile(ap):
            return ap[:, :, :].to_broadcast([P, NTILE, E])

        def every_expert(ap):
            return ap[:, :, :].to_broadcast([P, NTILE, E])

        N_ROUTE = 5 + 6

        def ve_route(ve):
            done = [0]

            def step(ins):
                ins.then_inc(S["rt_step"], 1)
                done[0] += 1
                ve.wait_ge(S["rt_step"], done[0])

            ve.wait_ge(ld["moe_const"], 16 * N_MOE_CONST)
            ve.wait_ge(S["logit_ready"], NB)
            step(nc.vector.tensor_reduce(rt_max[:, :, :], logits[:, :, :], AX_X, ALU.max))
            step(nc.vector.tensor_tensor(rt_shift[:, :, :], logits[:, :, :], every_expert(rt_max), ALU.subtract))
            ve.wait_ge(S["rt_exp"], 1)
            step(nc.vector.tensor_reduce(rt_sum[:, :, :], rt_exp[:, :, :], AX_X, ALU.add))
            step(nc.vector.reciprocal(rt_inv[:, :, :], rt_sum[:, :, :]))
            step(nc.vector.tensor_tensor(score[:, :, :], rt_exp[:, :, :], every_expert(rt_inv), ALU.mult))
            nc.vector.tensor_copy(ones_b[:, :], moe_f32[:, 0:P])
            nc.vector.tensor_copy(upper_b[:, :], moe_f32[:, P:2 * P])
            nc.vector.tensor_copy(iota[:, :], moe_f32[:, 2 * P:2 * P + CAP])
            tiles = moe_f32[:, 2 * P + CAP:2 * P + CAP + NTILE].rearrange("p (t o) -> p t o", o=1)
            nc.vector.tensor_copy(info[:, :, :, 0], tiles.to_broadcast([P, NTILE, E]))
            part = moe_f32[:, 2 * P + CAP + NTILE:].rearrange("p (t o) -> p t o", o=1)
            nc.vector.tensor_copy(info[:, :, :, 1], part.to_broadcast([P, NTILE, E]))
            nc.vector.memset(cur[:, :, :], 0.0)
            step(nc.vector.tensor_copy(info[:, :, :, 2], score[:, :, :]))
            step(nc.vector.tensor_tensor(score_r1[:, :, :], score[:, :, :], info[:, :, :, 2], ALU.subtract))
            step(nc.vector.tensor_copy(info[:, :, :, 3], score_r1[:, :, :]))
            step(nc.vector.tensor_tensor(score_r2[:, :, :], score_r1[:, :, :], info[:, :, :, 3], ALU.subtract))
            step(nc.vector.tensor_copy(info[:, :, :, 4], score_r2[:, :, :]))

        def ac_route(ac):
            ac.wait_ge(S["rt_step"], 2)
            nc.scalar.activation(rt_exp[:, :, :], rt_shift[:, :, :], ACT.Exp).then_inc(S["rt_exp"], 1)

        def ve_threshold(ve):
            with ve.Fori(0, NBITS) as n:
                nc.vector.tensor_tensor(cand[:, 0, :].bitcast(I32), cur[:, 0, :].bitcast(I32), bits[:, bass.ds(n, 1), :],
                                        ALU.bitwise_or).then_inc(S["rank_step"], 1)
                ve.wait_ge(S["rank_step"], n * 4 + 1)
                nc.vector.tensor_tensor(flag[:, :, :], score[:, :, :], every_tile(cand), ALU.is_ge
                                        ).then_inc(S["flag_ready"], 1)
                ve.wait_ge(S["rank_count"], n + 1)
                nc.vector.tensor_reduce(count[:, :], ps_m[0][:, 0:P].rearrange("p (t e) -> p e t", t=NTILE),
                                        AX_X, ALU.add).then_inc(S["rank_step"], 1)
                ve.wait_ge(S["rank_step"], n * 4 + 2)
                nc.vector.scalar_tensor_tensor(kept[:, 0, :], count[:, :], float(CAP), cand[:, 0, :],
                                               ALU.is_ge, ALU.mult).then_inc(S["rank_step"], 1)
                ve.wait_ge(S["rank_step"], n * 4 + 3)
                nc.vector.tensor_tensor(cur[:, 0, :], cur[:, 0, :], kept[:, 0, :], ALU.max
                                        ).then_inc(S["rank_step"], 1)
                ve.wait_ge(S["rank_step"], n * 4 + 4)

        def pe_threshold(pe):
            pe.wait_ge(S["rt_step"], N_ROUTE - 1)
            with pe.Fori(0, NBITS) as n:
                pe.wait_ge(S["flag_ready"], n + 1)
                nc.tensor.matmul(ps_m[0][:, 0:P], ones_b[:, :], tok(flag), start=True, stop=True
                                 ).then_inc(S["rank_count"], 1)

        def pe_ranks(flags, last_sem):
            nc.tensor.matmul(ps_m[1][:, 0:P], upper_b[:, :], tok(flags), start=True, stop=False)
            for t in range(NTILE - 1):
                rest = NTILE - 1 - t
                ins = nc.tensor.matmul(ps_m[1][:, (t + 1) * E:P].rearrange("p (t e) -> p t e", e=E), ones_b[:, :],
                                       flags[:, t:t + 1, :].to_broadcast([P, rest, E]),
                                       start=False, stop=(rest == 1))
            ins.then_inc(last_sem, 1)

        def ve_slots(ve):
            n0 = 4 * NBITS
            done = [n0]

            def step(ins):
                ins.then_inc(S["rank_step"], 1)
                done[0] += 1
                ve.wait_ge(S["rank_step"], done[0])

            step(nc.vector.tensor_tensor(above[:, :, :], score[:, :, :], every_tile(cur), ALU.is_gt))
            step(nc.vector.tensor_tensor(equal[:, :, :], score[:, :, :], every_tile(cur), ALU.is_equal))
            ve.wait_ge(S["sel_out"], 2)
            step(nc.vector.tensor_reduce(count[:, :], ps_m[0][:, 0:P].rearrange("p (t e) -> p e t", t=NTILE),
                                         AX_X, ALU.add))
            step(nc.vector.tensor_scalar(room[:, 0, :], count[:, :], -1.0, float(CAP), ALU.mult, ALU.add))
            step(nc.vector.tensor_tensor(early[:, :, :], ps_m[1][:, 0:P].rearrange("p (t e) -> p t e", e=E),
                                         every_tile(room), ALU.is_lt))
            step(nc.vector.tensor_tensor(tied[:, :, :], early[:, :, :], equal[:, :, :], ALU.mult))
            step(nc.vector.tensor_tensor(chosen[:, :, :], tied[:, :, :], above[:, :, :], ALU.add))
            ve.wait_ge(S["slot_out"], 1)
            step(nc.vector.scalar_tensor_tensor(slot_1[:, :, :].rearrange("p t e -> p (t e)"), ps_m[1][:, 0:P], 1.0,
                                                tok(chosen), ALU.add, ALU.mult))
            nc.vector.tensor_scalar(slot[:, :, :], slot_1[:, :, :], -1.0, None, ALU.add).then_inc(S["slots_ready"], 1)
            ve.wait_ge(S["slots_ready"], 1)

        def pe_slots(pe):
            n0 = 4 * NBITS
            pe.wait_ge(S["rank_step"], n0 + 2)
            nc.tensor.matmul(ps_m[0][:, 0:P], ones_b[:, :], tok(above), start=True, stop=True).then_inc(S["sel_out"], 1)
            pe_ranks(equal, S["sel_out"])
            pe.wait_ge(S["rank_step"], n0 + 7)
            pe_ranks(chosen, S["slot_out"])

        def ve_gather(ve, e, par):
            wait(ve, S["comp_out"], e)
            for t in range(NTILE):
                ins = nc.vector.tensor_scalar(onehot[:, t, :], iota[:, :], slot[:, t, bass.ds(e, 1)], None, ALU.is_equal)
            ins.then_inc(S["onehot_ready"], 1)
            wait(ve, S["comp_out"], e + 1)
            nc.vector.tensor_copy(comp[:, :, :], ps_c[:, 0:ST * 8].rearrange("p (s c) -> p s c", c=8)
                                  ).then_inc(S["comp_copied"], 1)
            wait(ve, S["comp_copied"], e + 1)
            wait(ve, S["scattered"], (e - 1) * 16 * ST)
            nc.vector.scalar_tensor_tensor(idx[par][:, :], comp[:, :, 0], float(P), comp[:, :, 1],
                                           ALU.mult, ALU.add).then_inc(S["idx_ready"], 1)
            nc.vector.tensor_tensor(gate1[:, :], comp[:, :, 2], comp[:, :, 3], ALU.add).then_inc(S["gate_step"], 1)
            wait(ve, S["gate_step"], e + 1)
            nc.vector.tensor_tensor(gate[par][:, :], gate1[:, :], comp[:, :, 4], ALU.add).then_inc(S["gate_ready"], 1)

        def ve_bias(ve, e, par):
            for i in range(2):
                wait(ve, S["w2_out"], 2 * e + i + 1)
                wait(ve, S["y_gated"], 2 * e)
                nc.vector.tensor_tensor(y_e[:, 2 * i:2 * i + 2, :], ps_o[i][:, :].rearrange("p (s d) -> p s d", s=2),
                                        b2e[:, bass.ds(e, 1), :].to_broadcast([P, 2, D]), ALU.add
                                        ).then_inc(S["y_added"], 1)

        def pe_compact(pe, e):
            wait(pe, S["onehot_ready"], e + 1)
            wait(pe, S["comp_copied"], e)
            for st in range(ST):
                for t in range(NTILE):
                    ins = nc.tensor.matmul(ps_c[:, st * 8:st * 8 + 5], onehot[:, t, st * P:(st + 1) * P],
                                           info[:, t, bass.ds(e, 1), :].rearrange("p o c -> p (o c)"),
                                           start=(t == 0), stop=(t == NTILE - 1))
            ins.then_inc(S["comp_out"], 1)

        def pe_gathered(pe, e):
            wait(pe, S["gathered"], (e + 1) * 16 * ST)
            wait(pe, S["xT_ready"], e)
            for c in range(DC):
                for st in range(ST):
                    ins = nc.tensor.matmul(ps_m[c][:, st * P:(st + 1) * P], xg[:, st, c * P:(c + 1) * P], ident[:, :],
                                           start=True, stop=True, is_transpose=True)
            ins.then_inc(S["xg_T"], 1)

        def pe_expert(pe, e, more):
            wait(pe, S["xT_ready"], e + 1)
            wait(pe, ld["w1e"], 16 * e + 16)
            for hc in range(FC):
                wait(pe, S["act_done"], e * FC + max(hc - 2, 0))
                for c in range(DC):
                    ins = nc.tensor.matmul(ps_h[hc % 3][:, :], w1e[:, c, hc * P:(hc + 1) * P], xgT[:, c, :],
                                           start=(c == 0), stop=(c == DC - 1))
                ins.then_inc(S["w1_out"], 1)
            if more:
                pe_compact(pe, e + 1)
            wait(pe, ld["w2e"], 16 * e + 16)
            wait(pe, S["act_done"], (e + 1) * FC)
            for i in range(2):
                if i == 1 and more:
                    pe_gathered(pe, e + 1)
                wait(pe, S["y_added"], 2 * e)
                for st in (2 * i, 2 * i + 1):
                    for hc in range(FC):
                        ins = nc.tensor.matmul(ps_o[i][:, (st % 2) * D:(st % 2 + 1) * D],
                                               hid_e[:, hc, st * P:(st + 1) * P], w2e[:, hc, :],
                                               start=(hc == 0), stop=(hc == FC - 1))
                ins.then_inc(S["w2_out"], 1)

        def ac_transposed(ac, e):
            wait(ac, S["xg_T"], e + 1)
            for c in range(DC):
                ins = nc.scalar.copy(xgT[:, c, :], ps_m[c][:, :])
            ins.then_inc(S["xT_ready"], 1)

        def ac_expert(ac, e, par, more):
            for hc in range(FC):
                wait(ac, S["w1_out"], e * FC + hc + 1)
                nc.scalar.activation(hid_e[:, hc, :], ps_h[hc % 3][:, :], ACT.Gelu,
                                     bias=b1e[:, bass.ds(e, 1), hc:hc + 1].rearrange("p o c -> p (o c)")
                                     ).then_inc(S["act_done"], 1)
            if more:
                ac_transposed(ac, e + 1)
            wait(ac, S["gate_ready"], e + 1)
            wait(ac, S["scattered"], e * 16 * ST)
            for i in range(2):
                wait(ac, S["y_added"], 2 * e + i + 1)
                for st in (2 * i, 2 * i + 1):
                    ins = nc.scalar.activation(y_g[:, st, :], y_e[:, st, :], ACT.Copy, scale=gate[par][:, st:st + 1])
                ins.then_inc(S["y_gated"], 1)

        def po_gather(po, e, par):
            wait_apart(po, (S["idx_ready"], e + 1), (S["xg_T"], e))
            for st in range(ST):
                nc.gpsimd.indirect_dma_start(xg[:, st, :], None, normed_dram,
                                             bass.IndirectOffsetOnAxis(ap=idx[par][:, st:st + 1], axis=0)
                                             ).then_inc(S["gathered"], 16)

        def po_scatter(po, e, par):
            for st in range(ST):
                wait_apart(po, (S["y_gated"], 2 * e + st // 2 + 1), (S["scattered"], (e * ST + st) * 16))
                nc.gpsimd.indirect_dma_start(out, bass.IndirectOffsetOnAxis(ap=idx[par][:, st:st + 1], axis=0),
                                             y_g[:, st, :], None, compute_op=ALU.add).then_inc(S["scattered"], 16)

        def experts(eng, first, one):
            first()
            with eng.Fori(0, E // 2 - 1) as i:
                one(i * 2, 0, True)
                one(i * 2 + 1, 1, True)
            one(E - 2, 0, True)
            one(E - 1, 1, False)

        block = ctx.enter_context(nc.Block())

        @block.sync
        def _(sp):
            def load_a(b):
                wait(sp, scores_ready, seg_a_units(b - 1))
                sp.dma_start(ctxT[A][:, :, :], a["ctxT"][b]).then_inc(ld["ctxT_A"], 16)

            def load_va_mask(b):
                wait(sp, S["mask_ready"], b)
                sp.dma_start(mask_int[:, :, :], a["mask"][b]).then_inc(ld["mask"], 16)
                wait(sp, S["va_ready"], b)
                sp.dma_start(v_raw[A][:, :, :], a["ctx"][b]).then_inc(ld["v_A"], 16)

            def load_c(b):
                wait(sp, S["v_out"], b)
                sp.dma_start(ctxT[C][:, :, :], a["ctxT"][b]).then_inc(ld["ctxT_C"], 16)

            def load_bias(b, qt):
                if not (isinstance(b, int) and b == 0):
                    wait(sp, neg_ready, seg_c(b - 1).base + PAIRS * (qt + 1))
                sp.dma_start(bias_t[qt][:, :, :], a["bias"][b][:, qt]).then_inc(ld[f"bias{qt}"], 16)

            def store(f):
                wait(sp, S["x3_ready"], f + 1)
                sp.dma_start(out.rearrange("(b t p) d -> b p t d", p=P, t=QT)[f], xpair(f)).then_inc(S["stored_x"], 16)
                wait(sp, ln_done["R"], f + 1)
                sp.dma_start(normed_dram.rearrange("(b t p) d -> b p t d", p=P, t=QT)[f], nrm["R"][:, :, :]).then_inc(S["stored_n"], 16)

            sp.dma_start(x_all[:, 0:QT, :], a["x"][0]).then_inc(ld["x0"], 16)
            load_a(0)
            load_va_mask(0)
            for dst, src in ((cols, "cols"), (ident, "ident")):
                sp.dma_start(dst[:, :], a[src]).then_inc(ld["const"], 16)
            for n in range(4):
                sp.dma_start(rows[:, n, :], a["rows"][n:n + 1, :].to_broadcast([P, D])).then_inc(ld["const"], 16)
            for dst, src in ((w_b, "w_b"), (w_a, "w_a"), (had, "had"), (w_k, "w_k"), (w_v, "w_v"), (w_q, "w_q"),
                             (w_o, "w_o"), (w_1, "w_1"), (w_2, "w_2"), (w_r, "w_r")):
                sp.dma_start(dst[:, :, :], a[src]).then_inc(ld["w"], 16)
            sp.dma_start(x_all[:, QT:NTILE, :].rearrange("p (b t) d -> p b t d", t=QT),
                         a["x"][1:NB].rearrange("b p t d -> p b t d")).then_inc(ld["x"], 16)
            load_va_mask(1)
            load_c(0)
            for qt in range(QT):
                load_bias(0, qt)
            load_a(1)
            for dst, src, n in ((moe_f32, "moe_f32", 2), (bits, "bits", 3), (b1e, "b1e", 3)):
                sp.dma_start(dst[:, :] if n == 2 else dst[:, :, :], a[src]).then_inc(ld["moe_const"], 16)

            def iteration(b, finish=True, last_a=False):
                if not last_a:
                    load_va_mask(b + 2)
                load_c(b + 1)
                if finish:
                    store(b - 1)
                if not last_a:
                    load_a(b + 2)
                for qt in range(QT):
                    load_bias(b + 1, qt)

            iteration(0, finish=False)
            with sp.Fori(1, NB - 2) as b:
                iteration(b)
            iteration(NB - 2, last_a=True)
            store(NB - 2)
            wait(sp, exp_ready, TOTAL_UNITS)
            sp.dma_start(w1e[:, :, :], a["w1e"][0]).then_inc(ld["w1e"], 16)
            wait(sp, S["f2_out"], NB)
            sp.dma_start(w2e[:, :, :], a["w2e"][0]).then_inc(ld["w2e"], 16)
            store(NB - 1)
            sp.wait_ge(S["stored_x"], 16 * NB)
            for e in range(E):
                sp.dma_start(b2e[:, e, :], a["b2e"][e:e + 1, :].to_broadcast([P, D])).then_inc(ld["b2e"], 16)

            def next_weights(e):
                wait(sp, S["w1_out"], (e + 1) * FC)
                sp.dma_start(w1e[:, :, :], a["w1e"][e + 1]).then_inc(ld["w1e"], 16)
                wait(sp, S["w2_out"], 2 * e + 2)
                sp.dma_start(w2e[:, :, :], a["w2e"][e + 1]).then_inc(ld["w2e"], 16)

            with sp.Fori(0, E - 1) as e:
                next_weights(e)
            sp.wait_ge(S["stored_x"], 16 * NB)
            sp.wait_ge(S["stored_n"], 16 * NB)
            sp.wait_ge(S["scattered"], 16 * ST * E)

        @block.tensor
        def _(pe):
            pe.wait_ge(ld["const"], 16 * N_CONST)
            pe.wait_ge(ld["w"], 16 * N_WEIGHTS)
            pe_start(pe)
            layers(pe, pe_seg, pe_side1, pe_side2)
            pe_threshold(pe)
            pe_slots(pe)

            def first():
                pe_compact(pe, 0)
                pe_gathered(pe, 0)

            experts(pe, first, lambda e, par, more: pe_expert(pe, e, more))

        @block.vector
        def _(ve):
            ve.wait_ge(ld["const"], 16 * N_CONST)
            ve_start(ve)
            layers(ve, ve_seg, ve_side1, ve_side2)
            ve_route(ve)
            ve_threshold(ve)
            ve_slots(ve)

            def one(e, par, more):
                if more:
                    ve_gather(ve, e + 1, 1 - par)
                ve_bias(ve, e, par)

            ve.wait_ge(ld["b2e"], 16 * E)
            experts(ve, lambda: ve_gather(ve, 0, 0), one)

        @block.scalar
        def _(ac):
            ac.wait_ge(ld["const"], 16 * N_CONST)
            ac_start(ac)
            layers(ac, ac_seg, ac_side1, ac_side2)
            ac_route(ac)
            experts(ac, lambda: ac_transposed(ac, 0), lambda e, par, more: ac_expert(ac, e, par, more))

        @block.gpsimd
        def _(po):
            po.wait_ge(ld["const"], 16 * N_CONST)
            po_start(po)
            layers(po, po_seg, po_side1, po_side2)
            po.wait_ge(S["stored_x"], 16 * NB)
            po.wait_ge(S["stored_n"], 16 * NB)

            def one(e, par, more):
                if more:
                    po_gather(po, e + 1, 1 - par)
                po_scatter(po, e, par)

            experts(po, lambda: po_gather(po, 0, 0), one)


N_CONST, N_WEIGHTS, N_MOE_CONST = 6, 10, 3
TOTAL_UNITS = 2 * NB * UNITS


def kernel(**inputs):
    import concourse.bacc as bacc
    from concourse.bass_utils import run_bass_kernel_spmd

    i = {k: np.asarray(v) for k, v in inputs.items()}
    part = np.arange(P)
    even = np.where((part // DK) % 2 == 0, DK ** -0.5, 0.0)
    odd = DK ** -0.5 - even
    arrays = {
        "x": i["x"],
        "ctx": i["ctx_1024"],
        "ctxT": i["ctx_1024"].transpose(0, 2, 1),
        "bias": i["fside_Bx16xSxS2_0"],
        "mask": i["mask_Bx1xSxS2_ik1"][:, 0],
        "w_a": i["L0_xattn_W"].T,
        "had": hadamard(D),
        "w_b": i["L0_ffn_weight"],
        "w_q": i["L1_xattn_Wq"].T, "w_k": i["L1_xattn_Wk"].T, "w_v": i["L1_xattn_Wv"].T, "w_o": i["L1_xattn_Wo"].T,
        "w_1": i["L1_xattn_W1"].T, "w_2": i["L1_xattn_W2"].T, "w_r": i["L1_ffn_Wr"],
        "w1e": i["L1_ffn_W1"], "w2e": i["L1_ffn_W2"],
        "b1e": i["L1_ffn_b1"].reshape(E, FC, P).transpose(2, 0, 1),
        "b2e": i["L1_ffn_b2"],
        "rows": np.stack([i["L0_xattn_b"], i["L1_xattn_b2"], i["L1_xattn_g2"], i["L1_xattn_be2"]]),
        "cols": np.concatenate([np.stack([even, odd], 1).astype(np.float32), i["L1_xattn_g1"].reshape(DC, P).T,
                                i["L1_xattn_be1"].reshape(DC, P).T, i["L1_xattn_b1"].reshape(FC, P).T], 1),
        "ident": np.eye(P, dtype=np.float32),
        "bits": np.broadcast_to((1 << np.arange(NBITS - 1, -1, -1)).astype(np.int32)[None, :, None], (P, NBITS, E)),
        "moe_f32": np.concatenate([np.ones((P, P)), np.triu(np.ones((P, P)), 1),
                                   np.broadcast_to(np.arange(CAP), (P, CAP)),
                                   np.broadcast_to(np.arange(NTILE), (P, NTILE)), part[:, None]], 1).astype(np.float32),
    }
    arrays = {k: np.ascontiguousarray(v) for k, v in arrays.items()}
    nc = bacc.Bacc("TRN2", target_bir_lowering=False, num_devices=1)
    a = {k: nc.dram_tensor(f"in_{k}", v.shape, mybir.dt.from_np(v.dtype), kind="ExternalInput").ap() for k, v in arrays.items()}
    out = nc.dram_tensor("out", [NB * SEQ, D], F32, kind="ExternalOutput").ap()
    tokens = "b (t p) d -> b p t d"
    a["x"] = a["x"].rearrange(tokens, p=P)
    a["ctx"] = a["ctx"].rearrange(tokens, p=P)
    a["mask"] = a["mask"].rearrange(tokens, p=P)
    a["ctxT"] = a["ctxT"].rearrange("b (c p) s -> b p c s", p=P)
    a["bias"] = a["bias"].rearrange("b h (t p) k -> b p t h k", p=P)
    for k in ("w_a", "had", "w_b", "w_q", "w_k", "w_v", "w_o", "w_1", "w_2", "w_r"):
        a[k] = a[k].rearrange("(c p) n -> p c n", p=P)
    a["w1e"] = a["w1e"].rearrange("e (c p) n -> e p c n", p=P)
    a["w2e"] = a["w2e"].rearrange("e (c p) n -> e p c n", p=P)
    build(nc, a, out)
    r = run_bass_kernel_spmd(nc, [{f"in_{k}": v for k, v in arrays.items()}], core_ids=[0])
    return r.results[0]["out"].reshape(NB, SEQ, D)


def hadamard(n):
    h = np.ones((1, 1))
    while h.shape[0] < n:
        h = np.block([[h, h], [h, -h]])
    return (h * n ** -0.5).astype(np.float32)
```
